# Optimizing a Trainium2 kernel written in Bass

```python
import numpy as np
import jax
import jax.numpy as jnp

def _softmax(x, axis=-1):
    return jax.nn.softmax(x, axis=axis)

def _gelu(x):
    return jax.nn.gelu(x, approximate=True)

def _silu(x):
    return jax.nn.silu(x)

def _sigmoid(x):
    return jax.nn.sigmoid(x)

def _layernorm(x, axis=-1, eps=1e-05):
    m = jnp.mean(x, axis=axis, keepdims=True)
    v = jnp.var(x, axis=axis, keepdims=True)
    return (x - m) / jnp.sqrt(v + eps)

def _scatter_add(tgt, idx, src, axis=0):
    return tgt.at[idx].add(src)

def _segment_sum(src, seg, n):
    return jax.ops.segment_sum(src, seg, n)
kernel_name = 'mk_dlrm_tower_d1_rec_r8_820b29'

def setup_inputs(seed: int=0):
    np.random.seed(seed)
    _w = jnp.asarray

    def _rec_inputs():
        import jax
        import jax.numpy as jnp
        _tk = jax.random.key(seed)
        dense_ctx = jax.random.normal(jax.random.fold_in(_tk, 190), (512, 16), jnp.float32)
        ids = jnp.stack([jax.random.randint(jax.random.fold_in(_tk, 200 + f), (512,), 0, v, jnp.int32) for f, v in enumerate([125000, 1000, 12500, 12500, 1000, 1250, 1250, 12500, 12500, 1000, 12500, 1000, 1000, 1000, 1000, 1000, 1000, 1000, 12500, 12500, 1000, 1000, 1250, 1000, 12500, 1250, 12500])], axis=1)
        tbl_0 = 0.05 * jax.random.normal(jax.random.fold_in(_tk, 500 + 0), (125000, 128), jnp.float32)
        tbl_1 = 0.05 * jax.random.normal(jax.random.fold_in(_tk, 500 + 1), (1000, 128), jnp.float32)
        tbl_2 = 0.05 * jax.random.normal(jax.random.fold_in(_tk, 500 + 2), (12500, 128), jnp.float32)
        tbl_3 = 0.05 * jax.random.normal(jax.random.fold_in(_tk, 500 + 3), (12500, 128), jnp.float32)
        tbl_4 = 0.05 * jax.random.normal(jax.random.fold_in(_tk, 500 + 4), (1000, 128), jnp.float32)
        tbl_5 = 0.05 * jax.random.normal(jax.random.fold_in(_tk, 500 + 5), (1250, 128), jnp.float32)
        tbl_6 = 0.05 * jax.random.normal(jax.random.fold_in(_tk, 500 + 6), (1250, 128), jnp.float32)
        tbl_7 = 0.05 * jax.random.normal(jax.random.fold_in(_tk, 500 + 7), (12500, 128), jnp.float32)
        tbl_8 = 0.05 * jax.random.normal(jax.random.fold_in(_tk, 500 + 8), (12500, 128), jnp.float32)
        tbl_9 = 0.05 * jax.random.normal(jax.random.fold_in(_tk, 500 + 9), (1000, 128), jnp.float32)
        tbl_10 = 0.05 * jax.random.normal(jax.random.fold_in(_tk, 500 + 10), (12500, 128), jnp.float32)
        tbl_11 = 0.05 * jax.random.normal(jax.random.fold_in(_tk, 500 + 11), (1000, 128), jnp.float32)
        tbl_12 = 0.05 * jax.random.normal(jax.random.fold_in(_tk, 500 + 12), (1000, 128), jnp.float32)
        tbl_13 = 0.05 * jax.random.normal(jax.random.fold_in(_tk, 500 + 13), (1000, 128), jnp.float32)
        tbl_14 = 0.05 * jax.random.normal(jax.random.fold_in(_tk, 500 + 14), (1000, 128), jnp.float32)
        tbl_15 = 0.05 * jax.random.normal(jax.random.fold_in(_tk, 500 + 15), (1000, 128), jnp.float32)
        tbl_16 = 0.05 * jax.random.normal(jax.random.fold_in(_tk, 500 + 16), (1000, 128), jnp.float32)
        tbl_17 = 0.05 * jax.random.normal(jax.random.fold_in(_tk, 500 + 17), (1000, 128), jnp.float32)
        tbl_18 = 0.05 * jax.random.normal(jax.random.fold_in(_tk, 500 + 18), (12500, 128), jnp.float32)
        tbl_19 = 0.05 * jax.random.normal(jax.random.fold_in(_tk, 500 + 19), (12500, 128), jnp.float32)
        tbl_20 = 0.05 * jax.random.normal(jax.random.fold_in(_tk, 500 + 20), (1000, 128), jnp.float32)
        tbl_21 = 0.05 * jax.random.normal(jax.random.fold_in(_tk, 500 + 21), (1000, 128), jnp.float32)
        tbl_22 = 0.05 * jax.random.normal(jax.random.fold_in(_tk, 500 + 22), (1250, 128), jnp.float32)
        tbl_23 = 0.05 * jax.random.normal(jax.random.fold_in(_tk, 500 + 23), (1000, 128), jnp.float32)
        tbl_24 = 0.05 * jax.random.normal(jax.random.fold_in(_tk, 500 + 24), (12500, 128), jnp.float32)
        tbl_25 = 0.05 * jax.random.normal(jax.random.fold_in(_tk, 500 + 25), (1250, 128), jnp.float32)
        tbl_26 = 0.05 * jax.random.normal(jax.random.fold_in(_tk, 500 + 26), (12500, 128), jnp.float32)
        _rk = jax.random.fold_in(_tk, 7)
        W_top1 = 0.0521996 * jax.random.normal(jax.random.fold_in(_tk, 801), (367, 512), jnp.float32)
        W_top2 = 0.0441942 * jax.random.normal(jax.random.fold_in(_tk, 802), (512, 256), jnp.float32)
        W_top3 = 0.0625 * jax.random.normal(jax.random.fold_in(_tk, 803), (256, 1), jnp.float32)
        b_top1 = jnp.zeros((512,), jnp.float32)
        b_top2 = jnp.zeros((256,), jnp.float32)
        return (dense_ctx, ids, tbl_0, tbl_1, tbl_2, tbl_3, tbl_4, tbl_5, tbl_6, tbl_7, tbl_8, tbl_9, tbl_10, tbl_11, tbl_12, tbl_13, tbl_14, tbl_15, tbl_16, tbl_17, tbl_18, tbl_19, tbl_20, tbl_21, tbl_22, tbl_23, tbl_24, tbl_25, tbl_26, W_top1, b_top1, W_top2, b_top2, W_top3)
    dense_ctx, ids, tbl_0, tbl_1, tbl_2, tbl_3, tbl_4, tbl_5, tbl_6, tbl_7, tbl_8, tbl_9, tbl_10, tbl_11, tbl_12, tbl_13, tbl_14, tbl_15, tbl_16, tbl_17, tbl_18, tbl_19, tbl_20, tbl_21, tbl_22, tbl_23, tbl_24, tbl_25, tbl_26, W_top1, b_top1, W_top2, b_top2, W_top3 = _rec_inputs()

    def _L0_rec_setup():
        import jax, jax.numpy as jnp
        import numpy as np

        def _tri_indices(num_feas):
            return np.array([i * num_feas + j for j in range(1, num_feas) for i in range(j)], dtype=np.int32)
        key = jax.random.key(seed)
        batch, num_feas, embed_dim = (2048, 27, 128)
        inputs = jax.random.normal(key, (batch, num_feas, embed_dim), dtype=jnp.float32)
        return {'inputs': inputs, 'num_feas': num_feas}
    _L0_rec_all = _L0_rec_setup()
    _L0_rec_in = {k: v for k, v in _L0_rec_all.items() if k in ()}
    del _L0_rec_all
    return {'dense_ctx': dense_ctx, 'ids': ids, 'tbl_0': tbl_0, 'tbl_1': tbl_1, 'tbl_2': tbl_2, 'tbl_3': tbl_3, 'tbl_4': tbl_4, 'tbl_5': tbl_5, 'tbl_6': tbl_6, 'tbl_7': tbl_7, 'tbl_8': tbl_8, 'tbl_9': tbl_9, 'tbl_10': tbl_10, 'tbl_11': tbl_11, 'tbl_12': tbl_12, 'tbl_13': tbl_13, 'tbl_14': tbl_14, 'tbl_15': tbl_15, 'tbl_16': tbl_16, 'tbl_17': tbl_17, 'tbl_18': tbl_18, 'tbl_19': tbl_19, 'tbl_20': tbl_20, 'tbl_21': tbl_21, 'tbl_22': tbl_22, 'tbl_23': tbl_23, 'tbl_24': tbl_24, 'tbl_25': tbl_25, 'tbl_26': tbl_26, 'W_top1': W_top1, 'b_top1': b_top1, 'W_top2': W_top2, 'b_top2': b_top2, 'W_top3': W_top3}

def reference(dense_ctx, ids, tbl_0, tbl_1, tbl_2, tbl_3, tbl_4, tbl_5, tbl_6, tbl_7, tbl_8, tbl_9, tbl_10, tbl_11, tbl_12, tbl_13, tbl_14, tbl_15, tbl_16, tbl_17, tbl_18, tbl_19, tbl_20, tbl_21, tbl_22, tbl_23, tbl_24, tbl_25, tbl_26, W_top1, b_top1, W_top2, b_top2, W_top3):
    import jax
    import jax.numpy as jnp

    def _L0_rec_ref(inputs, num_feas):
        import jax, jax.numpy as jnp
        import numpy as np

        def _tri_indices(num_feas):
            return np.array([i * num_feas + j for j in range(1, num_feas) for i in range(j)], dtype=np.int32)
        dot = jnp.einsum('bnd,bmd->bnm', inputs, inputs)
        idx = jnp.asarray(_tri_indices(num_feas))
        flat = dot.reshape(inputs.shape[0], num_feas * num_feas)
        return flat[:, idx]
    e = jnp.stack([tbl_0[ids[:, 0]], tbl_1[ids[:, 1]], tbl_2[ids[:, 2]], tbl_3[ids[:, 3]], tbl_4[ids[:, 4]], tbl_5[ids[:, 5]], tbl_6[ids[:, 6]], tbl_7[ids[:, 7]], tbl_8[ids[:, 8]], tbl_9[ids[:, 9]], tbl_10[ids[:, 10]], tbl_11[ids[:, 11]], tbl_12[ids[:, 12]], tbl_13[ids[:, 13]], tbl_14[ids[:, 14]], tbl_15[ids[:, 15]], tbl_16[ids[:, 16]], tbl_17[ids[:, 17]], tbl_18[ids[:, 18]], tbl_19[ids[:, 19]], tbl_20[ids[:, 20]], tbl_21[ids[:, 21]], tbl_22[ids[:, 22]], tbl_23[ids[:, 23]], tbl_24[ids[:, 24]], tbl_25[ids[:, 25]], tbl_26[ids[:, 26]]], axis=1)
    z = _L0_rec_ref(e, 27)
    z = z.reshape(z.shape[0], -1)
    h = jnp.concatenate([z, dense_ctx], axis=1)
    h = jnp.maximum(h @ W_top1 + b_top1, 0.0)
    h = jnp.maximum(h @ W_top2 + b_top2, 0.0)
    y = h @ W_top3
    return y

_drawn_inputs = setup_inputs


def setup_inputs(seed=0):
    import zlib

    import numpy as np

    out = dict(_drawn_inputs(seed))
    spreads = {'b_top1': (0.0, 0.1), 'b_top2': (0.0, 0.1)}
    factors = {}
    for name, (base, spread) in spreads.items():
        noise = np.random.default_rng([zlib.crc32(name.encode()), seed]).standard_normal(out[name].shape)
        drawn = base * np.exp(spread * noise) if base else spread * noise
        out[name] = jnp.asarray(drawn.astype(out[name].dtype))
    for name, factor in factors.items():
        out[name] = (out[name] * factor).astype(out[name].dtype)
    return out
```

```python
import numpy as np
import concourse.bass as bass
from concourse import mybir
from contextlib import ExitStack

F32, F32R, I32 = mybir.dt.float32, mybir.dt.float32r, mybir.dt.int32
ALU = mybir.AluOpType
RELU, ABS = mybir.ActivationFunctionType.Relu, mybir.ActivationFunctionType.Abs

B, F, D = 512, 27, 128
DENSE = 16
P = 128
TILES = B // P
Q = 4
G = P // Q
SLOT = 32
PAIRS = F * (F - 1) // 2
N1, N2 = 512, 256
K1 = PAIRS + DENSE
KC = [(0, 128), (128, 128), (256, K1 - 256)]
C1, C2 = N1 // P, N2 // P

VOCAB = [125000, 1000, 12500, 12500, 1000, 1250, 1250, 12500, 12500, 1000, 12500, 1000, 1000, 1000,
         1000, 1000, 1000, 1000, 12500, 12500, 1000, 1000, 1250, 1000, 12500, 1250, 12500]
SMALL = min(VOCAB)
CHUNKS = 8
ROWP = SMALL // CHUNKS
BATCH_SIZES = [1, 2, 2, 2, 2]
BATCHES = len(BATCH_SIZES)
BATCH_START = [sum(BATCH_SIZES[:n]) for n in range(BATCHES + 1)]
BATCH = max(BATCH_SIZES)
ONEHOT_TABLES = sum(BATCH_SIZES)
_small = [f for f in range(F) if VOCAB[f] == SMALL][:ONEHOT_TABLES]
SLOT_TABLE = [f for f in range(F) if f not in _small] + _small
GATHERED = F - ONEHOT_TABLES
GROUPS = [(s, min(4, GATHERED - s)) for s in range(0, GATHERED, 4)]

HALF = (F - 1) // 2
PITCH = 64
RING = 5
ACT_CHUNKS = (6,)
LO_AFTER = 5
EARLY = 2
WARMUP = 15

WHOLE = [slice(0, CHUNKS * D)]
HALVES = [slice(0, CHUNKS * D // 2), slice(CHUNKS * D // 2, CHUNKS * D)]


def by_act(n, c):
    return n > 0 and c in ACT_CHUNKS


def made_count(n, c):
    return sum(by_act(m, d) == by_act(n, c) for m in range(n + 1) for d in range(CHUNKS) if (m, d) <= (n, c))


def parts_split(n, j=0, half=1):
    return half + 1 if n == 0 else BATCH_START[n] + j + 2


def pair_rows():
    rows = []
    for k in range(HALF):
        for j in (HALF + 1 + k, HALF - k):
            for i in range(j):
                a, b = sorted((SLOT_TABLE[i], SLOT_TABLE[j]))
                rows.append(b * (b - 1) // 2 + a)
    return rows + list(range(PAIRS, K1))


def dlrm_tower(nc, ids_gather, ids_onehot, dense, tables, w1, b1, w2, b2, w3, out):
    ctx = ExitStack()
    with ctx:
        def sb(name, shape, dt=F32):
            return ctx.enter_context(nc.sbuf_tensor(name, shape, dt))

        def sem(name):
            return ctx.enter_context(nc.semaphore(name))

        ident = sb("ident", [P, P])
        rowid = sb("rowid", [P, CHUNKS], I32)
        rowidf = sb("rowidf", [P, CHUNKS])
        idx = sb("idx", [P, TILES, GATHERED], I32)
        ids_all = sb("ids_all", [P, ONEHOT_TABLES * B], I32)
        table_raw = [sb(f"table_raw{i}", [P, BATCH, CHUNKS * D]) for i in range(2)]
        table_hi = [sb(f"table_hi{i}", [P, BATCH, CHUNKS * D], F32R) for i in range(2)]
        table_lo = [sb(f"table_lo{i}", [P, BATCH, CHUNKS * D], F32R) for i in range(2)]
        onehot = sb("onehot", [P, RING, BATCH * B], F32R)
        rows = [sb(f"rows{i}", [P, GATHERED, D]) for i in range(2)]
        eT = sb("eT", [P, B, SLOT])
        gram = [sb(f"gram{i}", [P, F, G]) for i in range(2)]
        blocks = sb("blocks", [P, HALF * (PITCH + 1) + HALF + 1])
        z = sb("z", [P, TILES, K1])
        zT = sb("zT", [P, 3, P])
        w1_sb = sb("w1_sb", [P, 3, N1])
        w2_sb = sb("w2_sb", [P, C1, N2])
        w3_sb = sb("w3_sb", [P, C2])
        b1_sb = sb("b1_sb", [P, C1])
        b2_sb = sb("b2_sb", [P, C2])
        h1 = sb("h1", [P, C1, P])
        h2 = sb("h2", [P, C2, P])
        y = sb("y", [1, B])

        bank = [ctx.enter_context(nc.psum_tensor(f"bank{i}", [P, 512], F32)) for i in range(8)]
        lookup_bank = [bank[0:2], bank[6:8]]
        gram_bank = bank[0:2]
        rows_bank = bank[4:6]
        zT_bank = bank[2]
        h1_bank = [bank[3], bank[6]]
        h2_bank = [bank[7], bank[3]]
        y_bank = bank[7]

        distance = sb("distance", [P, BATCH * B])
        one = sb("one", [P, 1])

        ident_zeroed = sem("ident_zeroed")
        ident_made = sem("ident_made")
        act_started = sem("act_started")
        rowid_made = sem("rowid_made")
        rowid_float = sem("rowid_float")
        idx_loaded = sem("idx_loaded")
        ids_loaded = [sem(f"ids_loaded{n}") for n in range(BATCHES)]
        raw_loaded = [[sem(f"raw_loaded{i}_{j}") for j in range(BATCH)] for i in range(2)]
        dense_loaded = sem("dense_loaded")
        w1_loaded = sem("w1_loaded")
        w23_loaded = sem("w23_loaded")
        padding_zeroed = sem("padding_zeroed")
        hi_made = sem("hi_made")
        lo_made = sem("lo_made")
        one_made = sem("one_made")
        distance_made = sem("distance_made")
        onehot_made_dve = sem("onehot_made_dve")
        onehot_made_act = sem("onehot_made_act")
        onehot_used = sem("onehot_used")
        batch_stored_act = sem("batch_stored_act")
        batch_stored_dve = sem("batch_stored_dve")
        rows_gathered = [[sem(f"rows_gathered{i}_{g}") for g in range(len(GROUPS))] for i in range(2)]
        rows_turned = sem("rows_turned")
        rows_stored = sem("rows_stored")
        gram_ready = sem("gram_ready")
        gram_stored_dve = sem("gram_stored_dve")
        gram_stored_act = sem("gram_stored_act")
        blocks_long = sem("blocks_long")
        blocks_short = sem("blocks_short")
        z_packed = sem("z_packed")
        z_turned = sem("z_turned")
        zT_stored = sem("zT_stored")
        h1_ready = sem("h1_ready")
        h1_stored = sem("h1_stored")
        h2_ready = sem("h2_ready")
        h2_stored = sem("h2_stored")
        y_ready = sem("y_ready")
        y_stored = sem("y_stored")
        out_written = sem("out_written")

        NG = len(GROUPS)
        ROUNDS = G // Q

        block = ctx.enter_context(nc.Block())

        @block.sync
        def _(sp):
            def load_ids(n):
                i0, i1 = BATCH_START[n], BATCH_START[n + 1]
                sp.dma_start(ids_all[:, i0 * B:i1 * B],
                             ids_onehot[i0:i1, :].rearrange("f b -> (f b)").partition_broadcast(P)
                             ).then_inc(ids_loaded[n], 16)

            def load_batch(n):
                i0, i1 = BATCH_START[n], BATCH_START[n + 1]
                if n == 0:
                    load_ids(n)
                for j in range(i1 - i0):
                    src = tables[GATHERED + i0 + j].rearrange("(p c) d -> p (c d)", c=CHUNKS)
                    for a, b in ((0, 112), (112, ROWP)):
                        sp.dma_start(table_raw[n % 2][a:b, j, :], src[a:b, :]).then_inc(raw_loaded[n % 2][j], 16)
                if n > 0:
                    load_ids(n)

            sp.dma_start(idx[:, :, :], ids_gather).then_inc(idx_loaded, 16)
            load_batch(0)
            load_batch(1)
            for n in range(2, BATCHES):
                sp.wait_ge(hi_made, parts_split(n - 2, BATCH_SIZES[n - 2] - 1))
                sp.wait_ge(lo_made, parts_split(n - 2, BATCH_SIZES[n - 2] - 1))
                load_batch(n)
            sp.dma_start(z[:, :, PAIRS:K1], dense.rearrange("(t p) d -> p t d", p=P)).then_inc(dense_loaded, 16)
            sp.dma_start(w1_sb[:, 0:2, :], w1[0:2 * P, :].rearrange("(c p) n -> p c n", p=P)).then_inc(w1_loaded, 16)
            sp.dma_start(w1_sb[0:K1 - 2 * P, 2, :], w1[2 * P:K1, :]).then_inc(w1_loaded, 16)
            sp.dma_start(b1_sb[:, :], b1).then_inc(w1_loaded, 16)
            sp.dma_start(w2_sb[:, :, :], w2.rearrange("(c p) n -> p c n", p=P)).then_inc(w23_loaded, 16)
            sp.dma_start(b2_sb[:, :], b2).then_inc(w23_loaded, 16)
            sp.dma_start(w3_sb[:, :], w3).then_inc(w23_loaded, 16)
            sp.wait_ge(y_stored, TILES)
            sp.dma_start(out, y[0:1, :]).then_inc(out_written, 16)
            sp.wait_ge(out_written, 16)

        @block.gpsimd
        def _(pool):
            nc.gpsimd.memset(ident[:, :], 0.0).then_inc(ident_zeroed, 1)
            nc.gpsimd.iota(rowid[:, :], pattern=[[1, CHUNKS]], base=0, channel_multiplier=CHUNKS).then_inc(rowid_made, 1)
            pool.wait_ge(ident_zeroed, 1)
            nc.gpsimd.affine_select(out=ident[:, :], in_=ident[:, :], compare_op=ALU.not_equal, fill=1.0, base=0,
                                    pattern=[[-1, P]], channel_multiplier=1).then_inc(ident_made, 1)
            pool.wait_ge(idx_loaded, 16)
            for t in range(TILES):
                for g, (s0, width) in enumerate(GROUPS):
                    if t >= 2:
                        pool.wait_ge(rows_turned, NG * (t - 2) + g + 1)
                    for s in range(s0, s0 + width):
                        pool.indirect_dma_start(
                            out=rows[t % 2][:, s, :], out_offset=None, in_=tables[s][:, :],
                            in_offset=bass.IndirectOffsetOnAxis(ap=idx[:, t, s:s + 1], axis=0),
                        ).then_inc(rows_gathered[t % 2][g], 16)

        @block.scalar
        def _(act):
            def split_hi(n):
                if n >= 2:
                    act.wait_ge(onehot_used, CHUNKS * (n - 1))
                for j in range(BATCH_SIZES[n]):
                    act.wait_ge(raw_loaded[n % 2][j], 32 * sum(size > j for size in BATCH_SIZES[n % 2:n + 1:2]))
                    for cols in HALVES if n == 0 else WHOLE:
                        nc.scalar.copy(table_hi[n % 2][0:ROWP, j, cols],
                                       table_raw[n % 2][0:ROWP, j, cols]).then_inc(hi_made, 1)

            def make_onehot(n, c):
                width = BATCH_SIZES[n] * B
                act.wait_ge(ids_loaded[n], 16)
                nc.scalar.activation(distance[0:ROWP, 0:width], ids_all[0:ROWP, BATCH_START[n] * B:BATCH_START[n + 1] * B],
                                     ABS, bias=rowidf[0:ROWP, c:c + 1], scale=-1.0).then_inc(distance_made, 1)
                act.wait_ge(distance_made, made_count(n, c))
                act.wait_ge(onehot_used, CHUNKS * n + c - RING + 1)
                nc.scalar.activation(onehot[0:ROWP, (CHUNKS * n + c) % RING, 0:width], distance[0:ROWP, 0:width],
                                     RELU, bias=one[0:ROWP, 0:1], scale=-1.0).then_inc(onehot_made_act, 1)

            def store_batch(n):
                act.wait_ge(onehot_used, CHUNKS * (n + 1))
                for j in range(BATCH_SIZES[n]):
                    slot = GATHERED + BATCH_START[n] + j
                    nc.scalar.copy(eT[:, :, slot], lookup_bank[n % 2][j][:, :]).then_inc(batch_stored_act, 1)

            def store_rows(t, g):
                s0, width = GROUPS[g]
                n = NG * t + g
                act.wait_ge(rows_turned, n + 1)
                nc.scalar.copy(eT[:, t * P:(t + 1) * P, s0:s0 + width].rearrange("p b s -> p s b"),
                               rows_bank[n % 2][:, 0:width * P].rearrange("p (s b) -> p s b", b=P)).then_inc(rows_stored, 1)

            def store_gram(t):
                if t >= 2:
                    act.wait_ge(blocks_short, t - 1)
                for r in range(ROUNDS):
                    n = ROUNDS * t + r
                    act.wait_ge(gram_ready, n + 1)
                    for q in (2, 3):
                        src = gram_bank[n % 2][32 * q:32 * q + 32, 0:Q * Q * F].rearrange("p (g s j) -> p g s j", g=Q, s=Q)
                        nc.scalar.copy(gram[t % 2][32 * q:32 * q + 32, :, Q * r:Q * r + Q].rearrange("p j g -> p g j"),
                                       src[:, :, q, :]).then_inc(gram_stored_act, 1)
                    if r == 0 and t >= 2:
                        store_y(t - 2)

            def layers(t):
                def between(g):
                    if t + 2 < TILES and g < NG:
                        store_rows(t + 2, g)

                if t == 0:
                    act.wait_ge(w1_loaded, 48)
                for c in range(C1):
                    act.wait_ge(h1_ready, C1 * t + c + 1)
                    nc.scalar.activation(h1[:, c, :], h1_bank[c % 2][:, 0:P], RELU,
                                         bias=b1_sb[:, c:c + 1]).then_inc(h1_stored, 1)
                    between(c)
                if t == 0:
                    act.wait_ge(w23_loaded, 48)
                for m in range(C2):
                    act.wait_ge(h2_ready, C2 * t + m + 1)
                    nc.scalar.activation(h2[:, m, :], h2_bank[m][:, 0:P], RELU,
                                         bias=b2_sb[:, m:m + 1]).then_inc(h2_stored, 1)
                    between(C1 + m)

            def store_y(t):
                act.wait_ge(y_ready, t + 1)
                nc.scalar.copy(y[0:1, t * P:(t + 1) * P], y_bank[0:1, 0:P]).then_inc(y_stored, 1)

            act.wait_ge(one_made, 1)
            nc.scalar.activation(distance[:, 0:1], one[:, 0:1], RELU).then_inc(act_started, 1)
            split_hi(0)
            split_hi(1)
            act.wait_ge(act_started, 1)
            act.wait_ge(rowid_float, 1)
            for n in range(BATCHES):
                if n > 0:
                    if n + 1 < BATCHES:
                        split_hi(n + 1)
                    store_batch(n - 1)
                    for c in ACT_CHUNKS:
                        make_onehot(n, c)
                if n == BATCHES - 2:
                    for g in range(EARLY):
                        store_rows(0, g)
            for g in range(EARLY, NG):
                store_rows(0, g)
            store_gram(0)
            for g in range(NG):
                store_rows(1, g)
            for t in range(1, TILES):
                store_gram(t)
                layers(t - 1)
            store_y(TILES - 2)
            layers(TILES - 1)
            store_y(TILES - 1)

        @block.vector
        def _(dve):
            nc.vector.memset(one[:, :], 1.0).then_inc(one_made, 1)
            dve.wait_ge(rowid_made, 1)
            nc.vector.tensor_copy(rowidf[:, :], rowid[:, :]).then_inc(rowid_float, 1)
            nc.vector.memset(eT[:, :, F:SLOT], 0.0).then_inc(padding_zeroed, 1)

            def split_lo(n, j, half=None):
                cols = WHOLE[0] if half is None else HALVES[half]
                dve.wait_ge(hi_made, parts_split(n, j, 1 if half is None else half))
                nc.vector.tensor_tensor(table_lo[n % 2][0:ROWP, j, cols], table_raw[n % 2][0:ROWP, j, cols],
                                        table_hi[n % 2][0:ROWP, j, cols].bitcast(F32), ALU.subtract).then_inc(lo_made, 1)

            def make_onehot(n, c):
                i = CHUNKS * n + c
                if c == 0:
                    dve.wait_ge(ids_loaded[n], 16)
                if i >= RING:
                    dve.wait_ge(onehot_used, i - RING + 1)
                nc.vector.tensor_scalar(onehot[0:ROWP, i % RING, 0:BATCH_SIZES[n] * B],
                                        ids_all[0:ROWP, BATCH_START[n] * B:BATCH_START[n + 1] * B],
                                        rowidf[0:ROWP, c:c + 1], None, ALU.is_equal).then_inc(onehot_made_dve, 1)

            def store_gram(t):
                for r in range(ROUNDS):
                    n = ROUNDS * t + r
                    dve.wait_ge(gram_ready, n + 1)
                    for q in (0, 1):
                        src = gram_bank[n % 2][32 * q:32 * q + 32, 0:Q * Q * F].rearrange("p (g s j) -> p g s j", g=Q, s=Q)
                        nc.vector.tensor_copy(gram[t % 2][32 * q:32 * q + 32, :, Q * r:Q * r + Q].rearrange("p j g -> p g j"),
                                              src[:, :, q, :]).then_inc(gram_stored_dve, 1)

            def pack(t):
                dve.wait_ge(gram_stored_dve, 2 * ROUNDS * (t + 1))
                dve.wait_ge(gram_stored_act, 2 * ROUNDS * (t + 1))
                long = blocks[:, 0:HALF * PITCH].rearrange("p (k n) -> p k n", k=HALF)
                short = blocks[:, HALF + 1:HALF + 1 + HALF * (PITCH + 1)].rearrange("p (k n) -> p k n", k=HALF)
                nc.vector.transpose(long[:, :, 0:32], gram[t % 2][:, HALF + 1:F, :]).then_inc(blocks_long, 1)
                dve.wait_ge(blocks_long, t + 1)
                nc.vector.transpose(short[:, :, 0:32], gram[t % 2][:, HALF:0:-1, :]).then_inc(blocks_short, 1)
                dve.wait_ge(blocks_short, t + 1)
                nc.vector.tensor_copy(z[:, t, 0:PAIRS].rearrange("p (k n) -> p k n", k=HALF),
                                      long[:, :, 0:F]).then_inc(z_packed, 1)

            def store_z(t):
                dve.wait_ge(z_turned, t + 1)
                nc.vector.tensor_copy(zT[:, 0:2, :],
                                      zT_bank[:, 0:2 * P].rearrange("p (c b) -> p c b", b=P)).then_inc(zT_stored, 1)
                nc.vector.tensor_copy(zT[0:KC[2][1], 2, :], zT_bank[0:KC[2][1], 2 * P:3 * P]).then_inc(zT_stored, 1)

            dve.wait_ge(rowid_float, 1)
            for c in range(3):
                make_onehot(0, c)
            split_lo(0, 0, 0)
            make_onehot(0, 3)
            split_lo(0, 0, 1)
            make_onehot(0, 4)
            split_lo(1, 0)
            for c in range(5, CHUNKS):
                make_onehot(0, c)
            split_lo(1, 1)
            for n in range(1, BATCHES):
                todo = [c for c in range(CHUNKS) if not by_act(n, c)]
                for c in todo[:LO_AFTER]:
                    make_onehot(n, c)
                parts = range(BATCH_SIZES[n + 1]) if n + 1 < BATCHES else []
                for c in todo[LO_AFTER:]:
                    if parts:
                        split_lo(n + 1, parts[0])
                        parts = parts[1:]
                    make_onehot(n, c)
            dve.wait_ge(onehot_used, CHUNKS * BATCHES)
            for j in range(BATCH_SIZES[-1]):
                last = nc.vector.tensor_copy(eT[:, :, GATHERED + BATCH_START[-2] + j],
                                             lookup_bank[(BATCHES - 1) % 2][j][:, :])
            last.then_inc(batch_stored_dve, 1)
            store_gram(0)
            pack(0)
            store_z(0)
            for t in range(1, TILES):
                store_gram(t)
                pack(t)
                store_z(t)

        @block.tensor
        def _(pe):
            def lookup(n):
                for c in range(CHUNKS):
                    pe.wait_ge(onehot_made_act if by_act(n, c) else onehot_made_dve, made_count(n, c))
                    if n == 0 and c in (0, CHUNKS // 2):
                        pe.wait_ge(lo_made, parts_split(0, 0, c // (CHUNKS // 2)))
                    if c == 0 and n > 0:
                        pe.wait_ge(lo_made, parts_split(n, BATCH_SIZES[n] - 1))
                        if n >= 2:
                            pe.wait_ge(batch_stored_act, BATCH_START[n - 1])
                    for j in range(BATCH_SIZES[n]):
                        hot = onehot[0:ROWP, (CHUNKS * n + c) % RING, j * B:(j + 1) * B]
                        acc = lookup_bank[n % 2][j]
                        nc.tensor.matmul(acc[:, :], table_hi[n % 2][0:ROWP, j, c * D:(c + 1) * D], hot,
                                         start=(c == 0), stop=False)
                        last = nc.tensor.matmul(acc[:, :], table_lo[n % 2][0:ROWP, j, c * D:(c + 1) * D], hot,
                                                start=False, stop=(c == CHUNKS - 1))
                    last.then_inc(onehot_used, 1)

            def turn_rows(t, g):
                s0, width = GROUPS[g]
                n = NG * t + g
                pe.wait_ge(rows_gathered[t % 2][g], 16 * width * (t // 2 + 1))
                if n >= 2:
                    pe.wait_ge(rows_stored, n - 1)
                for s in range(width):
                    last = nc.tensor.transpose(rows_bank[n % 2][:, s * P:(s + 1) * P], rows[t % 2][:, s0 + s, :],
                                               ident[:, :])
                last.then_inc(rows_turned, 1)

            def dot_products(t):
                pe.wait_ge(rows_stored, NG * (t + 1))
                if t == 0:
                    pe.wait_ge(padding_zeroed, 1)
                    pe.wait_ge(batch_stored_act, BATCH_START[-2])
                    pe.wait_ge(batch_stored_dve, 1)
                for r in range(ROUNDS):
                    n = ROUNDS * t + r
                    if n >= 2:
                        pe.wait_ge(gram_stored_dve, 2 * (n - 1))
                        pe.wait_ge(gram_stored_act, 2 * (n - 1))
                    for i in range(Q):
                        b0 = t * P + (Q * r + i) * Q
                        last = nc.tensor.matmul(
                            gram_bank[n % 2][:, i * Q * F:(i + 1) * Q * F].rearrange("p (s j) -> p s j", j=F),
                            eT[:, b0:b0 + Q, :].rearrange("p s j -> p (s j)"), eT[:, b0:b0 + Q, 0:F],
                            start=True, stop=True)
                    last.then_inc(gram_ready, 1)
                    if r == 0 and t >= 2:
                        output(t - 2)

            def turn_z(t):
                pe.wait_ge(z_packed, t + 1)
                if t == 0:
                    pe.wait_ge(dense_loaded, 16)
                for c, (k0, k) in enumerate(KC):
                    last = nc.tensor.transpose(zT_bank[0:k, c * P:(c + 1) * P], z[:, t, k0:k0 + k], ident[:, :])
                last.then_inc(z_turned, 1)

            def layers(t):
                def between(g):
                    if t + 2 < TILES and g < NG:
                        turn_rows(t + 2, g)

                if t == 0:
                    pe.wait_ge(w1_loaded, 48)
                for n in range(C1):
                    if n >= 2:
                        pe.wait_ge(h1_stored, C1 * t + n - 1)
                    for c, (k0, k) in enumerate(KC):
                        if n == 0 and c != 1:
                            pe.wait_ge(zT_stored, 2 * t + 1 + c // 2)
                        last = nc.tensor.matmul(h1_bank[n % 2][:, 0:P], w1_sb[0:k, c, n * P:(n + 1) * P],
                                                zT[0:k, c, :], start=(c == 0), stop=(c == 2))
                    last.then_inc(h1_ready, 1)
                    between(n)
                if t + 1 < TILES:
                    turn_z(t + 1)
                if t == 0:
                    pe.wait_ge(w23_loaded, 48)
                else:
                    pe.wait_ge(y_stored, t)
                for m in range(C2):
                    for c in range(C1):
                        if m == 0:
                            pe.wait_ge(h1_stored, C1 * t + c + 1)
                        last = nc.tensor.matmul(h2_bank[m][:, 0:P], w2_sb[:, c, m * P:(m + 1) * P],
                                                h1[:, c, :], start=(c == 0), stop=(c == C1 - 1))
                    last.then_inc(h2_ready, 1)
                    between(C1 + m)

            def output(t):
                for m in range(C2):
                    pe.wait_ge(h2_stored, C2 * t + m + 1)
                    last = nc.tensor.matmul(y_bank[0:1, 0:P], w3_sb[:, m:m + 1], h2[:, m, :],
                                            start=(m == 0), stop=(m == C2 - 1))
                last.then_inc(y_ready, 1)

            pe.wait_ge(ident_made, 1)
            for _ in range(WARMUP):
                nc.tensor.matmul(zT_bank[:, 0:P], ident[:, :], ident[:, :], start=True, stop=True)
            for n in range(BATCHES):
                lookup(n)
                if n == BATCHES - 2:
                    for g in range(EARLY):
                        turn_rows(0, g)
            for g in range(EARLY, NG):
                turn_rows(0, g)
            dot_products(0)
            for g in range(NG):
                turn_rows(1, g)
            turn_z(0)
            for t in range(1, TILES):
                dot_products(t)
                layers(t - 1)
            output(TILES - 2)
            layers(TILES - 1)
            output(TILES - 1)


def kernel(**inputs):
    import concourse.bacc as bacc
    from concourse.bass_utils import run_bass_kernel_spmd

    ids = np.asarray(inputs["ids"])
    by_position = ids.reshape(TILES, Q, G, F)[:, :, :, SLOT_TABLE].transpose(2, 1, 0, 3).reshape(P, TILES, F)
    arrays = {
        "ids_gather": by_position[:, :, :GATHERED],
        "ids_onehot": by_position[:, :, GATHERED:].transpose(2, 1, 0).reshape(ONEHOT_TABLES, B),
        "dense": inputs["dense_ctx"],
        "w1": np.asarray(inputs["W_top1"])[pair_rows()],
        "b1": np.asarray(inputs["b_top1"]).reshape(C1, P).T,
        "w2": inputs["W_top2"],
        "b2": np.asarray(inputs["b_top2"]).reshape(C2, P).T,
        "w3": np.asarray(inputs["W_top3"]).reshape(C2, P).T,
    }
    for s, f in enumerate(SLOT_TABLE):
        arrays[f"table{s}"] = inputs[f"tbl_{f}"]
    arrays = {name: np.ascontiguousarray(a) for name, a in arrays.items()}

    nc = bacc.Bacc("TRN2", target_bir_lowering=False, num_devices=1)
    aps = {name: nc.dram_tensor(name, a.shape, mybir.dt.from_np(a.dtype), kind="ExternalInput").ap()
           for name, a in arrays.items()}
    out = nc.dram_tensor("out", (1, B), F32, kind="ExternalOutput").ap()
    dlrm_tower(nc, aps["ids_gather"], aps["ids_onehot"], aps["dense"], [aps[f"table{s}"] for s in range(F)],
               aps["w1"], aps["b1"], aps["w2"], aps["b2"], aps["w3"], out)
    r = run_bass_kernel_spmd(nc, [arrays], core_ids=[0])
    return r.results[0]["out"].reshape(B, 1)
```
